# Optimizing a Trainium2 kernel written in Bass

```python
import numpy as np
import jax
import jax.numpy as jnp

def _softmax(x, axis=-1):
    return jax.nn.softmax(x, axis=axis)

def _gelu(x):
    return jax.nn.gelu(x, approximate=True)

def _silu(x):
    return jax.nn.silu(x)

def _sigmoid(x):
    return jax.nn.sigmoid(x)

def _layernorm(x, axis=-1, eps=1e-05):
    m = jnp.mean(x, axis=axis, keepdims=True)
    v = jnp.var(x, axis=axis, keepdims=True)
    return (x - m) / jnp.sqrt(v + eps)

def _scatter_add(tgt, idx, src, axis=0):
    return tgt.at[idx].add(src)

def _segment_sum(src, seg, n):
    return jax.ops.segment_sum(src, seg, n)
kernel_name = 'mk_dlrm_tower_d1_rec_r8_fb736f'

def setup_inputs(seed: int=0):
    np.random.seed(seed)
    _w = jnp.asarray

    def _rec_inputs():
        import jax
        import jax.numpy as jnp
        _tk = jax.random.key(seed)
        dense_ctx = jax.random.normal(jax.random.fold_in(_tk, 190), (512, 16), jnp.float32)
        ids = jnp.stack([jax.random.randint(jax.random.fold_in(_tk, 200 + f), (512,), 0, v, jnp.int32) for f, v in enumerate([125000, 1250, 1250, 1000, 1250, 1000, 1000, 1000, 12500, 1250, 1250, 12500, 1250, 1250, 1000, 1250, 1000, 12500, 12500, 12500, 1000, 12500, 1000, 1250, 12500, 1000, 12500])], axis=1)
        tbl_0 = 0.05 * jax.random.normal(jax.random.fold_in(_tk, 500 + 0), (125000, 128), jnp.float32)
        tbl_1 = 0.05 * jax.random.normal(jax.random.fold_in(_tk, 500 + 1), (1250, 128), jnp.float32)
        tbl_2 = 0.05 * jax.random.normal(jax.random.fold_in(_tk, 500 + 2), (1250, 128), jnp.float32)
        tbl_3 = 0.05 * jax.random.normal(jax.random.fold_in(_tk, 500 + 3), (1000, 128), jnp.float32)
        tbl_4 = 0.05 * jax.random.normal(jax.random.fold_in(_tk, 500 + 4), (1250, 128), jnp.float32)
        tbl_5 = 0.05 * jax.random.normal(jax.random.fold_in(_tk, 500 + 5), (1000, 128), jnp.float32)
        tbl_6 = 0.05 * jax.random.normal(jax.random.fold_in(_tk, 500 + 6), (1000, 128), jnp.float32)
        tbl_7 = 0.05 * jax.random.normal(jax.random.fold_in(_tk, 500 + 7), (1000, 128), jnp.float32)
        tbl_8 = 0.05 * jax.random.normal(jax.random.fold_in(_tk, 500 + 8), (12500, 128), jnp.float32)
        tbl_9 = 0.05 * jax.random.normal(jax.random.fold_in(_tk, 500 + 9), (1250, 128), jnp.float32)
        tbl_10 = 0.05 * jax.random.normal(jax.random.fold_in(_tk, 500 + 10), (1250, 128), jnp.float32)
        tbl_11 = 0.05 * jax.random.normal(jax.random.fold_in(_tk, 500 + 11), (12500, 128), jnp.float32)
        tbl_12 = 0.05 * jax.random.normal(jax.random.fold_in(_tk, 500 + 12), (1250, 128), jnp.float32)
        tbl_13 = 0.05 * jax.random.normal(jax.random.fold_in(_tk, 500 + 13), (1250, 128), jnp.float32)
        tbl_14 = 0.05 * jax.random.normal(jax.random.fold_in(_tk, 500 + 14), (1000, 128), jnp.float32)
        tbl_15 = 0.05 * jax.random.normal(jax.random.fold_in(_tk, 500 + 15), (1250, 128), jnp.float32)
        tbl_16 = 0.05 * jax.random.normal(jax.random.fold_in(_tk, 500 + 16), (1000, 128), jnp.float32)
        tbl_17 = 0.05 * jax.random.normal(jax.random.fold_in(_tk, 500 + 17), (12500, 128), jnp.float32)
        tbl_18 = 0.05 * jax.random.normal(jax.random.fold_in(_tk, 500 + 18), (12500, 128), jnp.float32)
        tbl_19 = 0.05 * jax.random.normal(jax.random.fold_in(_tk, 500 + 19), (12500, 128), jnp.float32)
        tbl_20 = 0.05 * jax.random.normal(jax.random.fold_in(_tk, 500 + 20), (1000, 128), jnp.float32)
        tbl_21 = 0.05 * jax.random.normal(jax.random.fold_in(_tk, 500 + 21), (12500, 128), jnp.float32)
        tbl_22 = 0.05 * jax.random.normal(jax.random.fold_in(_tk, 500 + 22), (1000, 128), jnp.float32)
        tbl_23 = 0.05 * jax.random.normal(jax.random.fold_in(_tk, 500 + 23), (1250, 128), jnp.float32)
        tbl_24 = 0.05 * jax.random.normal(jax.random.fold_in(_tk, 500 + 24), (12500, 128), jnp.float32)
        tbl_25 = 0.05 * jax.random.normal(jax.random.fold_in(_tk, 500 + 25), (1000, 128), jnp.float32)
        tbl_26 = 0.05 * jax.random.normal(jax.random.fold_in(_tk, 500 + 26), (12500, 128), jnp.float32)
        _rk = jax.random.fold_in(_tk, 7)
        W_top1 = 0.0521996 * jax.random.normal(jax.random.fold_in(_tk, 801), (367, 512), jnp.float32)
        W_top2 = 0.0441942 * jax.random.normal(jax.random.fold_in(_tk, 802), (512, 256), jnp.float32)
        W_top3 = 0.0625 * jax.random.normal(jax.random.fold_in(_tk, 803), (256, 1), jnp.float32)
        b_top1 = jnp.zeros((512,), jnp.float32)
        b_top2 = jnp.zeros((256,), jnp.float32)
        return (dense_ctx, ids, tbl_0, tbl_1, tbl_2, tbl_3, tbl_4, tbl_5, tbl_6, tbl_7, tbl_8, tbl_9, tbl_10, tbl_11, tbl_12, tbl_13, tbl_14, tbl_15, tbl_16, tbl_17, tbl_18, tbl_19, tbl_20, tbl_21, tbl_22, tbl_23, tbl_24, tbl_25, tbl_26, W_top1, b_top1, W_top2, b_top2, W_top3)
    dense_ctx, ids, tbl_0, tbl_1, tbl_2, tbl_3, tbl_4, tbl_5, tbl_6, tbl_7, tbl_8, tbl_9, tbl_10, tbl_11, tbl_12, tbl_13, tbl_14, tbl_15, tbl_16, tbl_17, tbl_18, tbl_19, tbl_20, tbl_21, tbl_22, tbl_23, tbl_24, tbl_25, tbl_26, W_top1, b_top1, W_top2, b_top2, W_top3 = _rec_inputs()

    def _L0_rec_setup():
        import jax, jax.numpy as jnp
        import numpy as np
        NUM_FEAS = 27
        key = jax.random.key(seed)
        inputs = jax.random.normal(key, (4096, NUM_FEAS, 128), dtype=jnp.float32)
        return {'inputs': inputs}
    _L0_rec_all = _L0_rec_setup()
    _L0_rec_in = {k: v for k, v in _L0_rec_all.items() if k in ()}
    del _L0_rec_all
    return {'dense_ctx': dense_ctx, 'ids': ids, 'tbl_0': tbl_0, 'tbl_1': tbl_1, 'tbl_2': tbl_2, 'tbl_3': tbl_3, 'tbl_4': tbl_4, 'tbl_5': tbl_5, 'tbl_6': tbl_6, 'tbl_7': tbl_7, 'tbl_8': tbl_8, 'tbl_9': tbl_9, 'tbl_10': tbl_10, 'tbl_11': tbl_11, 'tbl_12': tbl_12, 'tbl_13': tbl_13, 'tbl_14': tbl_14, 'tbl_15': tbl_15, 'tbl_16': tbl_16, 'tbl_17': tbl_17, 'tbl_18': tbl_18, 'tbl_19': tbl_19, 'tbl_20': tbl_20, 'tbl_21': tbl_21, 'tbl_22': tbl_22, 'tbl_23': tbl_23, 'tbl_24': tbl_24, 'tbl_25': tbl_25, 'tbl_26': tbl_26, 'W_top1': W_top1, 'b_top1': b_top1, 'W_top2': W_top2, 'b_top2': b_top2, 'W_top3': W_top3}

def reference(dense_ctx, ids, tbl_0, tbl_1, tbl_2, tbl_3, tbl_4, tbl_5, tbl_6, tbl_7, tbl_8, tbl_9, tbl_10, tbl_11, tbl_12, tbl_13, tbl_14, tbl_15, tbl_16, tbl_17, tbl_18, tbl_19, tbl_20, tbl_21, tbl_22, tbl_23, tbl_24, tbl_25, tbl_26, W_top1, b_top1, W_top2, b_top2, W_top3):
    import jax
    import jax.numpy as jnp

    def _L0_rec_ref(inputs):
        import jax, jax.numpy as jnp
        import numpy as np
        NUM_FEAS = 27
        n = inputs.shape[1]
        dot = jnp.einsum('bnd,bmd->bnm', inputs, inputs)
        iu, ju = jnp.triu_indices(n, k=1)
        return dot[:, iu, ju]
    e = jnp.stack([tbl_0[ids[:, 0]], tbl_1[ids[:, 1]], tbl_2[ids[:, 2]], tbl_3[ids[:, 3]], tbl_4[ids[:, 4]], tbl_5[ids[:, 5]], tbl_6[ids[:, 6]], tbl_7[ids[:, 7]], tbl_8[ids[:, 8]], tbl_9[ids[:, 9]], tbl_10[ids[:, 10]], tbl_11[ids[:, 11]], tbl_12[ids[:, 12]], tbl_13[ids[:, 13]], tbl_14[ids[:, 14]], tbl_15[ids[:, 15]], tbl_16[ids[:, 16]], tbl_17[ids[:, 17]], tbl_18[ids[:, 18]], tbl_19[ids[:, 19]], tbl_20[ids[:, 20]], tbl_21[ids[:, 21]], tbl_22[ids[:, 22]], tbl_23[ids[:, 23]], tbl_24[ids[:, 24]], tbl_25[ids[:, 25]], tbl_26[ids[:, 26]]], axis=1)
    z = _L0_rec_ref(e)
    z = z.reshape(z.shape[0], -1)
    h = jnp.concatenate([z, dense_ctx], axis=1)
    h = jnp.maximum(h @ W_top1 + b_top1, 0.0)
    h = jnp.maximum(h @ W_top2 + b_top2, 0.0)
    y = h @ W_top3
    return y

_drawn_inputs = setup_inputs


def setup_inputs(seed=0):
    import zlib

    import numpy as np

    out = dict(_drawn_inputs(seed))
    spreads = {'b_top1': (0.0, 0.1), 'b_top2': (0.0, 0.1)}
    factors = {}
    for name, (base, spread) in spreads.items():
        noise = np.random.default_rng([zlib.crc32(name.encode()), seed]).standard_normal(out[name].shape)
        drawn = base * np.exp(spread * noise) if base else spread * noise
        out[name] = jnp.asarray(drawn.astype(out[name].dtype))
    for name, factor in factors.items():
        out[name] = (out[name] * factor).astype(out[name].dtype)
    return out
```

```python
from contextlib import ExitStack

import concourse.bass as bass
from concourse import mybir
from concourse.bass import IndirectOffsetOnAxis

P = 128
QUAD = 32
NQ = P // QUAD


def slots(features):
    return -(-features // NQ)


def dlrm_tower(nc, dense_t, ids, tables, w1p, w2, small, y):
    fp32 = mybir.dt.float32
    ALU = mybir.AluOpType
    ACT = mybir.ActivationFunctionType

    F = len(tables)
    D = tables[0].shape[1]
    B = ids.shape[0]
    TILES = B // P
    DENSE = dense_t.shape[0]
    JQ = slots(F)
    H1, H2 = w2.shape
    C1, C2 = H1 // P, H2 // P

    GF = 3
    GROUPS = F // GF
    FOURS = P // NQ
    CHUNK = 8
    CHUNKS = FOURS // CHUNK

    with ExitStack() as ctx:
        def sb(name, shape, dt=fp32):
            return ctx.enter_context(nc.sbuf_tensor(name, shape, dt))

        def pb(name, shape):
            return ctx.enter_context(nc.psum_tensor(name, shape, fp32))

        def sem(name):
            return ctx.enter_context(nc.semaphore(name))

        ids_sb = sb("ids_sb", [P, TILES, F], mybir.dt.int32)
        ident = sb("ident", [P, P])
        rows = sb("rows", [P, TILES, F, D])
        emb_t = sb("emb_t", [D, 2, FOURS, NQ, QUAD])
        pairs = sb("pairs", [P, 2, JQ, P])
        w1_sb = sb("w1_sb", [P, JQ, H1])
        w2_sb = sb("w2_sb", [P, C1, H2])
        small_sb = sb("small_sb", [P, C1 + 2 * C2])
        b1_sb, b2_sb, w3_sb = small_sb[:, :C1], small_sb[:, C1:C1 + C2], small_sb[:, C1 + C2:]
        h1 = sb("h1", [P, C1, P])
        h2 = sb("h2", [P, C2, P])
        y_sb = sb("y_sb", [1, B])

        rows_t_ps = [pb(f"rows_t_ps{k}", [P, 512]) for k in range(2)]
        gram_ps = [pb(f"gram_ps{k}", [P, CHUNK, P]) for k in range(2)]
        h1_ps = pb("h1_ps", [P, C1, P])
        h2_ps = pb("h2_ps", [P, 512])
        y_ps = h2_ps[0:1, C2 * P:(C2 + 1) * P]

        ids_in = sem("ids_in")
        dense_in = sem("dense_in")
        w1_in = sem("w1_in")
        w2_in = sem("w2_in")
        small_in = sem("small_in")
        ident_clear = sem("ident_clear")
        ident_ready = sem("ident_ready")
        gathered = [[sem(f"gathered_{t}_{g}") for g in range(GROUPS)] for t in range(TILES)]
        padded = sem("padded")
        rows_transposed = sem("rows_transposed")
        emb_t_ready = sem("emb_t_ready")
        gram_done = sem("gram_done")
        pairs_by_dve = sem("pairs_by_dve")
        pairs_by_act = sem("pairs_by_act")
        h1_done = sem("h1_done")
        h1_ready = sem("h1_ready")
        h2_done = sem("h2_done")
        h2_ready = sem("h2_ready")
        y_done = sem("y_done")
        y_ready = sem("y_ready")
        y_out = sem("y_out")

        DVE_MOVES = [(q, r) for q in (0, 1) for r in range(NQ)]
        ACT_MOVES = [(q, r) for q in (2, 3) for r in range(NQ)]

        def move_pairs(t, c, q, r):
            first = 1 if r == 0 else 0
            n = (F - 1 - r) // NQ + 1 - first
            j0 = r + NQ * first
            grams = gram_ps[(t * CHUNKS + c) % 2]
            src = grams[QUAD * q:QUAD * (q + 1), :, QUAD * q + j0:QUAD * q + j0 + NQ * (n - 1) + 1:NQ]
            s0 = QUAD * q + CHUNK * c
            dst = pairs[QUAD * r:QUAD * (r + 1), t % 2, first:first + n, s0:s0 + CHUNK]
            return dst, src.rearrange("p s j -> p j s")

        block = ctx.enter_context(nc.Block())

        @block.sync
        def _(sp):
            sp.dma_start(ids_sb[:], ids.rearrange("(t p) f -> p t f", p=P)).then_inc(ids_in, 16)
            sp.dma_start(small_sb[:], small).then_inc(small_in, 16)
            sp.dma_start(w1_sb[:], w1p.rearrange("s p n -> p s n")).then_inc(w1_in, 16)
            sp.dma_start(w2_sb[:], w2.rearrange("(c p) n -> p c n", p=P)).then_inc(w2_in, 16)
            sp.wait_ge(padded, 1)
            for t in range(TILES):
                if t >= 2:
                    sp.wait_ge(h1_done, t - 1)
                    sp.wait_ge(dense_in, 16 * t)
                sp.dma_start(pairs[0:DENSE, t % 2, 0, :], dense_t[:, t * P:(t + 1) * P]).then_inc(dense_in, 16)
            sp.wait_ge(y_ready, TILES)
            sp.dma_start(y, y_sb[:]).then_inc(y_out, 16)
            sp.wait_ge(y_out, 16)

        @block.gpsimd
        def _(pool):
            nc.gpsimd.memset(ident[:], 0.0).then_inc(ident_clear, 1)
            pool.wait_ge(ident_clear, 1)
            nc.gpsimd.affine_select(out=ident[:], in_=ident[:], compare_op=ALU.not_equal, fill=1.0, base=0,
                                    pattern=[[-1, P]], channel_multiplier=1).then_inc(ident_ready, 1)
            pool.wait_ge(ids_in, 16)
            for t in range(TILES):
                for f in range(F):
                    nc.gpsimd.indirect_dma_start(
                        rows[:, t, f, :], None, tables[f],
                        IndirectOffsetOnAxis(ap=ids_sb[:, t, f:f + 1], axis=0),
                    ).then_inc(gathered[t][f // GF], 16)

        @block.tensor
        def _(pe):
            for t in range(TILES):
                for g in range(GROUPS):
                    n = t * GROUPS + g
                    pe.wait_ge(gathered[t][g], 16 * GF)
                    if n == 0:
                        pe.wait_ge(ident_ready, 1)
                    if n >= 2:
                        pe.wait_ge(emb_t_ready, n - 1)
                    for k in range(GF):
                        last = nc.tensor.transpose(rows_t_ps[n % 2][:, k * P:(k + 1) * P],
                                                   rows[:, t, g * GF + k, :], ident[:])
                    last.then_inc(rows_transposed, 1)
                pe.wait_ge(emb_t_ready, GROUPS * (t + 1))
                if t == 0:
                    pe.wait_ge(padded, 1)
                for c in range(CHUNKS):
                    n = t * CHUNKS + c
                    if n >= 2:
                        pe.wait_ge(pairs_by_dve, n - 1)
                        pe.wait_ge(pairs_by_act, n - 1)
                    for s in range(CHUNK):
                        four = emb_t[:, t % 2, c * CHUNK + s, :, :]
                        last = nc.tensor.matmul(gram_ps[n % 2][:, s, :], four.rearrange("d q f -> d (q f)"),
                                                four.rearrange("d q f -> d (q f)"), start=True, stop=True)
                    last.then_inc(gram_done, 1)
                pe.wait_ge(pairs_by_dve, CHUNKS * (t + 1))
                pe.wait_ge(pairs_by_act, CHUNKS * (t + 1))
                pe.wait_ge(dense_in, 16 * (t + 1) if t >= 2 else 32)
                if t == 0:
                    pe.wait_ge(w1_in, 16)
                else:
                    pe.wait_ge(h1_ready, t)
                for c in range(C1):
                    for s in range(JQ):
                        last = nc.tensor.matmul(h1_ps[:, c, :], w1_sb[:, s, c * P:(c + 1) * P],
                                                pairs[:, t % 2, s, :], start=(s == 0), stop=(s == JQ - 1))
                last.then_inc(h1_done, 1)
                pe.wait_ge(h1_ready, t + 1)
                if t == 0:
                    pe.wait_ge(w2_in, 16)
                    pe.wait_ge(small_in, 16)
                else:
                    pe.wait_ge(y_ready, t)
                for c in range(C2):
                    for k in range(C1):
                        last = nc.tensor.matmul(h2_ps[:, c * P:(c + 1) * P], w2_sb[:, k, c * P:(c + 1) * P],
                                                h1[:, k, :], start=(k == 0), stop=(k == C1 - 1))
                last.then_inc(h2_done, 1)
                pe.wait_ge(h2_ready, t + 1)
                for k in range(C2):
                    last = nc.tensor.matmul(y_ps, w3_sb[:, k:k + 1], h2[:, k, :],
                                            start=(k == 0), stop=(k == C2 - 1))
                last.then_inc(y_done, 1)

        @block.vector
        def _(dve):
            nc.vector.memset(emb_t[:, :, :, :, F:QUAD], 0.0)
            nc.vector.memset(pairs[:, :, 0, :], 0.0)
            nc.vector.memset(pairs[:, :, JQ - 1, :], 0.0).then_inc(padded, 1)
            dve.wait_ge(padded, 1)
            for t in range(TILES):
                if t >= 2:
                    dve.wait_ge(gram_done, CHUNKS * (t - 1))
                for g in range(GROUPS):
                    n = t * GROUPS + g
                    dve.wait_ge(rows_transposed, n + 1)
                    dst = emb_t[:, t % 2, :, :, g * GF:(g + 1) * GF].rearrange("d s q f -> d f q s")
                    src = rows_t_ps[n % 2][:, 0:GF * P].rearrange("d (f q s) -> d f q s", f=GF, q=NQ)
                    nc.vector.tensor_copy(dst, src).then_inc(emb_t_ready, 1)
                if t >= 2:
                    dve.wait_ge(h1_done, t - 1)
                for c in range(CHUNKS):
                    dve.wait_ge(gram_done, t * CHUNKS + c + 1)
                    for q, r in DVE_MOVES:
                        dst, src = move_pairs(t, c, q, r)
                        last = nc.vector.tensor_copy(dst, src)
                    last.then_inc(pairs_by_dve, 1)

        @block.scalar
        def _(act):
            act.wait_ge(padded, 1)
            act.wait_ge(small_in, 16)
            for t in range(TILES):
                if t >= 2:
                    act.wait_ge(h1_done, t - 1)
                for c in range(CHUNKS):
                    act.wait_ge(gram_done, t * CHUNKS + c + 1)
                    for q, r in ACT_MOVES:
                        dst, src = move_pairs(t, c, q, r)
                        last = nc.scalar.copy(dst, src)
                    last.then_inc(pairs_by_act, 1)
                act.wait_ge(h1_done, t + 1)
                if t >= 1:
                    act.wait_ge(h2_done, t)
                for c in range(C1):
                    last = nc.scalar.activation(h1[:, c, :], h1_ps[:, c, :], ACT.Relu, bias=b1_sb[:, c:c + 1])
                last.then_inc(h1_ready, 1)
                act.wait_ge(h2_done, t + 1)
                if t >= 1:
                    act.wait_ge(y_done, t)
                for c in range(C2):
                    last = nc.scalar.activation(h2[:, c, :], h2_ps[:, c * P:(c + 1) * P], ACT.Relu,
                                                bias=b2_sb[:, c:c + 1])
                last.then_inc(h2_ready, 1)
                act.wait_ge(y_done, t + 1)
                nc.scalar.copy(y_sb[:, t * P:(t + 1) * P], y_ps).then_inc(y_ready, 1)


def kernel(**inputs):
    import numpy as np
    import concourse.bacc as bacc
    from concourse.bass_utils import run_bass_kernel_spmd

    F = inputs["ids"].shape[1]
    w1 = np.asarray(inputs["W_top1"])
    w1p = np.zeros((slots(F), NQ, QUAD, w1.shape[1]), w1.dtype)
    i, j = np.triu_indices(F, k=1)
    w1p[j // NQ, j % NQ, i] = w1[:len(i)]
    w1p[0, 0, :w1.shape[0] - len(i)] = w1[len(i):]

    laid = {"dense_t": np.ascontiguousarray(np.asarray(inputs["dense_ctx"]).T),
            "ids": np.ascontiguousarray(inputs["ids"]),
            **{f"tbl_{f}": np.ascontiguousarray(inputs[f"tbl_{f}"]) for f in range(F)},
            "w1p": w1p.reshape(slots(F), P, -1),
            "w2": np.ascontiguousarray(inputs["W_top2"]),
            "small": np.concatenate([np.asarray(inputs[k]).reshape(-1, P)
                                     for k in ("b_top1", "b_top2", "W_top3")]).T.copy()}

    nc = bacc.Bacc("TRN2", target_bir_lowering=False, num_devices=1)
    ap = {k: nc.dram_tensor(k + "_dram", v.shape, mybir.dt.from_np(v.dtype), kind="ExternalInput").ap()
          for k, v in laid.items()}
    B = laid["ids"].shape[0]
    y = nc.dram_tensor("y_dram", (1, B), mybir.dt.float32, kind="ExternalOutput").ap()
    dlrm_tower(nc, ap["dense_t"], ap["ids"], [ap[f"tbl_{f}"] for f in range(F)], ap["w1p"], ap["w2"],
               ap["small"], y)
    r = run_bass_kernel_spmd(nc, [{k + "_dram": v for k, v in laid.items()}], core_ids=[0])
    return r.results[0]["y_dram"].reshape(B, 1)
```

```python
from contextlib import ExitStack

import concourse.bass as bass
from concourse import mybir
from concourse.bass import IndirectOffsetOnAxis

P = 128
QUAD = 32
NQ = P // QUAD
HOT_ROWS = 1000
HOT_MAX = 6
HOT_PARTS = 125


def feature_order(table_rows):
    hot = [f for f, v in enumerate(table_rows) if v == HOT_ROWS][:HOT_MAX]
    return hot + [f for f in range(len(table_rows)) if f not in hot], len(hot)


def slots(features):
    return -(-features // NQ)


def dlrm_tower(nc, dense_t, ids, hot_ids, tables, w1p, w2, small, y):
    fp32 = mybir.dt.float32
    fp32r = mybir.dt.float32r
    i32 = mybir.dt.int32
    ALU = mybir.AluOpType
    ACT = mybir.ActivationFunctionType

    F = len(tables)
    ORDER, HOT = feature_order([tb.shape[0] for tb in tables])
    D = tables[0].shape[1]
    B = ids.shape[0]
    TILES = B // P
    DENSE = dense_t.shape[0]
    JQ = slots(F)
    H1, H2 = w2.shape
    C1, C2 = H1 // P, H2 // P
    HC = HOT_ROWS // HOT_PARTS

    GROUPS = [list(range(a, min(a + 4, F))) for a in range(HOT, F, 4)]
    NG = len(GROUPS)
    SETS = P // NQ

    NJ = F - 1
    CHUNK = 8
    CHUNKS = SETS // CHUNK

    def chunks(t):
        return [(t * CHUNKS + k, k * CHUNK) for k in range(CHUNKS)]

    with ExitStack() as ctx:
        def sb(name, shape, dt=fp32):
            return ctx.enter_context(nc.sbuf_tensor(name, shape, dt))

        def pb(name, shape):
            return ctx.enter_context(nc.psum_tensor(name, shape, fp32))

        def sem(name):
            return ctx.enter_context(nc.semaphore(name))

        ids_sb = sb("ids_sb", [P, TILES, F], i32)
        ident = sb("ident", [P, P])
        hot_row_i = sb("hot_row_i", [P, HC], i32)
        hot_row = sb("hot_row", [P, HC])
        hot_ids_sb = sb("hot_ids_sb", [HOT_PARTS, HOT, B], i32)
        table = sb("table", [HOT_PARTS, 2, HC, D])
        table_hi = sb("table_hi", [HOT_PARTS, 2, HC, D], fp32r)
        table_lo = sb("table_lo", [HOT_PARTS, 2, HC, D], fp32r)
        RING = 8
        onehot = sb("onehot", [HOT_PARTS, RING, B], fp32r)
        rows = sb("rows", [P, TILES, F - HOT, D])
        emb_t = sb("emb_t", [D, TILES, SETS, NQ, QUAD])
        pairs = sb("pairs", [P, 2, JQ, P])
        w1_sb = sb("w1_sb", [P, JQ, H1])
        w2_sb = sb("w2_sb", [P, C1, H2])
        small_sb = sb("small_sb", [P, C1 + 2 * C2])
        b1_sb, b2_sb, w3_sb = small_sb[:, :C1], small_sb[:, C1:C1 + C2], small_sb[:, C1 + C2:]
        h1 = sb("h1", [P, C1, P])
        h2 = sb("h2", [P, C2, P])
        y_sb = sb("y_sb", [1, B])

        rows_t_ps = [pb(f"rows_t_ps{k}", [P, 512]) for k in range(2)]
        gram_ps = [pb(f"gram_ps{k}", [P, CHUNK, P]) for k in range(2)]
        hot_ps = [ps.rearrange("p s x -> p (s x)")[:, 0:B] for ps in gram_ps]
        h1_ps = pb("h1_ps", [P, C1, P])
        h2_ps = pb("h2_ps", [P, 512])
        y_ps = h2_ps[0:1, C2 * P:(C2 + 1) * P]

        ids_in = sem("ids_in")
        hot_ids_in = [sem(f"hot_ids_in{k}") for k in range(2)]
        table_in = [sem(f"table_in{k}") for k in range(2)]
        dense_in = sem("dense_in")
        w1_in = sem("w1_in")
        w2_in = sem("w2_in")
        small_in = sem("small_in")
        ident_clear = sem("ident_clear")
        ident_ready = sem("ident_ready")
        hot_row_made = sem("hot_row_made")
        hot_row_ready = sem("hot_row_ready")
        table_hi_ready = sem("table_hi_ready")
        table_lo_ready = sem("table_lo_ready")
        onehot_ready = sem("onehot_ready")
        onehot_used = sem("onehot_used")
        hot_moved = sem("hot_moved")
        gathered = [[sem(f"gathered_{t}_{g}") for g in range(NG)] for t in range(TILES)]
        padded = sem("padded")
        rows_transposed = sem("rows_transposed")
        rows_moved = sem("rows_moved")
        gram_done = sem("gram_done")
        pairs_by_dve = sem("pairs_by_dve")
        pairs_by_act = sem("pairs_by_act")
        h1_done = sem("h1_done")
        h1_ready = sem("h1_ready")
        h2_done = sem("h2_done")
        h2_ready = sem("h2_ready")
        y_done = sem("y_done")
        y_ready = sem("y_ready")
        y_out = sem("y_out")

        HOT_LAG = HOT - NG

        def move_pairs(engine_copy, t, n, s0, quadrants):
            for q in quadrants:
                for r in range(NQ):
                    first = r if r else NQ
                    count = len(range(first, F, NQ))
                    x0 = q * NJ + first - 1
                    src = gram_ps[n % 2][QUAD * q:QUAD * (q + 1), :, x0:x0 + NQ * (count - 1) + 1:NQ]
                    a = QUAD * q + s0
                    dst = pairs[QUAD * r:QUAD * (r + 1), t % 2, first // NQ:first // NQ + count, a:a + CHUNK]
                    last = engine_copy(dst, src.rearrange("p s j -> p j s"))
            return last

        DVE_QUADRANTS, ACT_QUADRANTS = (0, 1), (2, 3)

        def move_rows(engine_copy, t, g):
            places = GROUPS[g]
            k = len(places)
            n = t * NG + g
            dst = emb_t[:, t, :, :, places[0]:places[0] + k].rearrange("d s q f -> d f q s")
            src = rows_t_ps[n % 2][:, 0:k * P].rearrange("d (f q s) -> d f q s", f=k, q=NQ)
            engine_copy(dst, src).then_inc(rows_moved, 1)

        block = ctx.enter_context(nc.Block())

        @block.sync
        def _(sp):
            sp.dma_start(ids_sb[:], ids.rearrange("(t p) f -> p t f", p=P)).then_inc(ids_in, 16)

            def load_table(h):
                if h >= 2:
                    sp.wait_ge(table_hi_ready, h - 1)
                    sp.wait_ge(table_lo_ready, h - 1)
                sp.dma_start(table[:, h % 2], tables[ORDER[h]].rearrange("(p c) d -> p c d", c=HC)
                             ).then_inc(table_in[h % 2], 16)

            load_table(0)
            sp.dma_start(hot_ids_sb[:, 0, :], hot_ids[0:1, :].to_broadcast([HOT_PARTS, B])
                         ).then_inc(hot_ids_in[0], 16)
            sp.dma_start(hot_ids_sb[:, 1:, :].rearrange("p h b -> p (h b)"),
                         hot_ids[1:, :].rearrange("(o h) b -> o (h b)", o=1).to_broadcast(
                             [HOT_PARTS, (HOT - 1) * B])).then_inc(hot_ids_in[1], 16)
            load_table(1)
            sp.dma_start(small_sb[:], small).then_inc(small_in, 16)
            sp.wait_ge(padded, 1)
            for t in range(2):
                sp.dma_start(pairs[0:DENSE, t, 0, :], dense_t[:, t * P:(t + 1) * P]).then_inc(dense_in, 16)
            for h in range(2, HOT):
                load_table(h)
            sp.dma_start(w1_sb[:], w1p.rearrange("s p n -> p s n")).then_inc(w1_in, 16)
            sp.dma_start(w2_sb[:], w2.rearrange("(c p) n -> p c n", p=P)).then_inc(w2_in, 16)
            for t in range(2, TILES):
                sp.wait_ge(h1_done, t - 1)
                sp.wait_ge(dense_in, 16 * t)
                sp.dma_start(pairs[0:DENSE, t % 2, 0, :], dense_t[:, t * P:(t + 1) * P]).then_inc(dense_in, 16)
            sp.wait_ge(y_ready, TILES)
            sp.dma_start(y, y_sb[:]).then_inc(y_out, 16)
            sp.wait_ge(y_out, 16)

        @block.gpsimd
        def _(pool):
            nc.gpsimd.iota(hot_row_i[:], pattern=[[1, HC]], base=0, channel_multiplier=HC
                           ).then_inc(hot_row_made, 1)
            nc.gpsimd.memset(ident[:], 0.0).then_inc(ident_clear, 1)
            pool.wait_ge(ident_clear, 1)
            nc.gpsimd.affine_select(out=ident[:], in_=ident[:], compare_op=ALU.not_equal, fill=1.0, base=0,
                                    pattern=[[-1, P]], channel_multiplier=1).then_inc(ident_ready, 1)
            pool.wait_ge(ids_in, 16)
            for t in range(TILES):
                for g in range(NG):
                    for place in GROUPS[g]:
                        f = ORDER[place]
                        nc.gpsimd.indirect_dma_start(
                            rows[:, t, place - HOT, :], None, tables[f],
                            IndirectOffsetOnAxis(ap=ids_sb[:, t, f:f + 1], axis=0),
                        ).then_inc(gathered[t][g], 16)

        @block.tensor
        def _(pe):
            def transpose_rows(t, g):
                n = t * NG + g
                pe.wait_ge(gathered[t][g], 16 * len(GROUPS[g]))
                if n >= 2:
                    pe.wait_ge(rows_moved, n - 1)
                for k, place in enumerate(GROUPS[g]):
                    last = nc.tensor.transpose(rows_t_ps[n % 2][:, k * P:(k + 1) * P],
                                               rows[:, t, place - HOT, :], ident[:])
                last.then_inc(rows_transposed, 1)

            pe.wait_ge(ident_ready, 1)
            for h in range(HOT):
                pe.wait_ge(table_lo_ready, h + 1)
                if h >= 2:
                    pe.wait_ge(hot_moved, h - 1)
                for c in range(HC):
                    n = h * HC + c
                    pe.wait_ge(onehot_ready, n + 1)
                    for part in (table_hi, table_lo):
                        last = nc.tensor.matmul(hot_ps[h % 2], part[:, h % 2, c, :], onehot[:, n % RING, :],
                                                start=(c == 0 and part is table_hi),
                                                stop=(c == HC - 1 and part is table_lo))
                    last.then_inc(onehot_used, 1)
                if h >= HOT_LAG:
                    transpose_rows(0, h - HOT_LAG)
            pe.wait_ge(hot_moved, HOT)
            pe.wait_ge(padded, 1)

            def gram(t):
                pe.wait_ge(rows_moved, NG * (t + 1))
                for n, s0 in chunks(t):
                    if n >= 2:
                        pe.wait_ge(pairs_by_dve, n - 1)
                        pe.wait_ge(pairs_by_act, n - 1)
                    for s in range(CHUNK):
                        four = emb_t[:, t, s0 + s, :, :]
                        last = nc.tensor.matmul(gram_ps[n % 2][:, s, 0:NQ * NJ],
                                                four.rearrange("d q f -> d (q f)"),
                                                four[:, :, 1:F], start=True, stop=True)
                    last.then_inc(gram_done, 1)

            def first_layer(t):
                pe.wait_ge(pairs_by_dve, CHUNKS * (t + 1))
                pe.wait_ge(pairs_by_act, CHUNKS * (t + 1))
                pe.wait_ge(dense_in, 16 * max(t + 1, 2))
                if t == 0:
                    pe.wait_ge(w1_in, 16)
                else:
                    pe.wait_ge(h1_ready, t)
                for c in range(C1):
                    for s in range(JQ):
                        last = nc.tensor.matmul(h1_ps[:, c, :], w1_sb[:, s, c * P:(c + 1) * P],
                                                pairs[:, t % 2, s, :], start=(s == 0), stop=(s == JQ - 1))
                    if c == C1 - 1:
                        last.then_inc(h1_done, 1)
                    if t < TILES - 1 and c < NG:
                        transpose_rows(t + 1, c)
                    if t >= 1 and c == 0:
                        third_layer(t - 1)
                if t < TILES - 1:
                    for g in range(C1, NG):
                        transpose_rows(t + 1, g)

            def second_layer(t):
                pe.wait_ge(h1_ready, t + 1)
                if t == 0:
                    pe.wait_ge(w2_in, 16)
                    pe.wait_ge(small_in, 16)
                else:
                    pe.wait_ge(y_ready, t)
                for c in range(C2):
                    for k in range(C1):
                        last = nc.tensor.matmul(h2_ps[:, c * P:(c + 1) * P], w2_sb[:, k, c * P:(c + 1) * P],
                                                h1[:, k, :], start=(k == 0), stop=(k == C1 - 1))
                last.then_inc(h2_done, 1)

            def third_layer(t):
                pe.wait_ge(h2_ready, t + 1)
                for k in range(C2):
                    last = nc.tensor.matmul(y_ps, w3_sb[:, k:k + 1], h2[:, k, :],
                                            start=(k == 0), stop=(k == C2 - 1))
                last.then_inc(y_done, 1)

            for t in range(TILES):
                gram(t)
                if t >= 1:
                    second_layer(t - 1)
                first_layer(t)
            second_layer(TILES - 1)
            third_layer(TILES - 1)

        @block.vector
        def _(dve):
            nc.vector.memset(emb_t[:, :, :, :, F:QUAD].rearrange("d t s q f -> d (t s q) f"), 0.0)
            nc.vector.memset(pairs[:, :, 0, :], 0.0)
            nc.vector.memset(pairs[:, :, JQ - 1, :], 0.0).then_inc(padded, 1)
            dve.wait_ge(hot_row_made, 1)
            nc.vector.tensor_copy(hot_row[:], hot_row_i[:]).then_inc(hot_row_ready, 1)
            dve.wait_ge(hot_row_ready, 1)
            dve.wait_ge(padded, 1)
            for h in range(HOT):
                dve.wait_ge(hot_ids_in[min(h, 1)], 16)
                for c in range(HC):
                    n = h * HC + c
                    if n >= RING:
                        dve.wait_ge(onehot_used, n - RING + 1)
                    nc.vector.tensor_scalar(onehot[:, n % RING, :], hot_ids_sb[:, h, :],
                                            hot_row[0:HOT_PARTS, c:c + 1], None, ALU.is_equal
                                            ).then_inc(onehot_ready, 1)
                    if c == 0:
                        dve.wait_ge(table_hi_ready, h + 1)
                        nc.vector.tensor_tensor(table_lo[:, h % 2], table[:, h % 2],
                                                table_hi[:, h % 2].bitcast(fp32), ALU.subtract
                                                ).then_inc(table_lo_ready, 1)
            for t in range(TILES):
                if t >= 1:
                    for g in range(NG):
                        dve.wait_ge(rows_transposed, t * NG + g + 1)
                        move_rows(nc.vector.tensor_copy, t, g)
                if t >= 2:
                    dve.wait_ge(h1_done, t - 1)
                for n, s0 in chunks(t):
                    dve.wait_ge(gram_done, n + 1)
                    move_pairs(nc.vector.tensor_copy, t, n, s0, DVE_QUADRANTS).then_inc(pairs_by_dve, 1)

        @block.scalar
        def _(act):
            for h in range(HOT):
                act.wait_ge(table_in[h % 2], 16 * (h // 2 + 1))
                if h >= 2:
                    act.wait_ge(onehot_used, HC * (h - 1))
                nc.scalar.copy(table_hi[:, h % 2], table[:, h % 2]).then_inc(table_hi_ready, 1)
                if h == 0:
                    act.wait_ge(padded, 1)
                if h >= 1:
                    act_move_hot = h - 1
                    act.wait_ge(onehot_used, HC * h)
                    nc.scalar.copy(emb_t[:, :, :, :, act_move_hot].rearrange("d t s q -> d t q s"),
                                   hot_ps[act_move_hot % 2].rearrange("d (t q s) -> d t q s", t=TILES, q=NQ)
                                   ).then_inc(hot_moved, 1)
                    if act_move_hot >= HOT_LAG:
                        act.wait_ge(rows_transposed, act_move_hot - HOT_LAG + 1)
                        move_rows(nc.scalar.copy, 0, act_move_hot - HOT_LAG)
            act.wait_ge(onehot_used, HC * HOT)
            nc.scalar.copy(emb_t[:, :, :, :, HOT - 1].rearrange("d t s q -> d t q s"),
                           hot_ps[(HOT - 1) % 2].rearrange("d (t q s) -> d t q s", t=TILES, q=NQ)
                           ).then_inc(hot_moved, 1)
            act.wait_ge(rows_transposed, NG)
            move_rows(nc.scalar.copy, 0, NG - 1)
            act.wait_ge(small_in, 16)

            def move_h2_and_y(t):
                act.wait_ge(h2_done, t + 1)
                if t >= 1:
                    act.wait_ge(y_done, t)
                for c in range(C2):
                    last = nc.scalar.activation(h2[:, c, :], h2_ps[:, c * P:(c + 1) * P], ACT.Relu,
                                                bias=b2_sb[:, c:c + 1])
                last.then_inc(h2_ready, 1)
                act.wait_ge(y_done, t + 1)
                nc.scalar.copy(y_sb[:, t * P:(t + 1) * P], y_ps).then_inc(y_ready, 1)

            for t in range(TILES):
                if t >= 2:
                    act.wait_ge(h1_done, t - 1)
                for n, s0 in chunks(t):
                    act.wait_ge(gram_done, n + 1)
                    move_pairs(nc.scalar.copy, t, n, s0, ACT_QUADRANTS).then_inc(pairs_by_act, 1)
                if t >= 1:
                    move_h2_and_y(t - 1)
                act.wait_ge(h1_done, t + 1)
                if t >= 1:
                    act.wait_ge(h2_done, t)
                for c in range(C1):
                    last = nc.scalar.activation(h1[:, c, :], h1_ps[:, c, :], ACT.Relu, bias=b1_sb[:, c:c + 1])
                last.then_inc(h1_ready, 1)
            move_h2_and_y(TILES - 1)


def kernel(**inputs):
    import numpy as np
    import concourse.bacc as bacc
    from concourse.bass_utils import run_bass_kernel_spmd

    F = inputs["ids"].shape[1]
    order, hot = feature_order([inputs[f"tbl_{f}"].shape[0] for f in range(F)])
    w1 = np.asarray(inputs["W_top1"])
    w1p = np.zeros((slots(F), NQ, QUAD, w1.shape[1]), w1.dtype)
    pair_row = np.zeros((F, F), int)
    i, j = np.triu_indices(F, k=1)
    pair_row[i, j] = pair_row[j, i] = np.arange(len(i))
    w1p[j // NQ, j % NQ, i] = w1[pair_row[np.asarray(order)[i], np.asarray(order)[j]]]
    w1p[0, 0, :w1.shape[0] - len(i)] = w1[len(i):]

    ids = np.asarray(inputs["ids"])
    laid = {"dense_t": np.ascontiguousarray(np.asarray(inputs["dense_ctx"]).T),
            "ids": np.ascontiguousarray(ids),
            "hot_ids": np.ascontiguousarray(ids.T[order[:hot]]),
            **{f"tbl_{f}": np.ascontiguousarray(inputs[f"tbl_{f}"]) for f in range(F)},
            "w1p": w1p.reshape(slots(F), P, -1),
            "w2": np.ascontiguousarray(inputs["W_top2"]),
            "small": np.concatenate([np.asarray(inputs[k]).reshape(-1, P)
                                     for k in ("b_top1", "b_top2", "W_top3")]).T.copy()}

    nc = bacc.Bacc("TRN2", target_bir_lowering=False, num_devices=1)
    ap = {k: nc.dram_tensor(k + "_dram", v.shape, mybir.dt.from_np(v.dtype), kind="ExternalInput").ap()
          for k, v in laid.items()}
    B = laid["ids"].shape[0]
    y = nc.dram_tensor("y_dram", (1, B), mybir.dt.float32, kind="ExternalOutput").ap()
    dlrm_tower(nc, ap["dense_t"], ap["ids"], ap["hot_ids"], [ap[f"tbl_{f}"] for f in range(F)], ap["w1p"],
               ap["w2"], ap["small"], y)
    r = run_bass_kernel_spmd(nc, [{k + "_dram": v for k, v in laid.items()}], core_ids=[0])
    return r.results[0]["y_dram"].reshape(B, 1)
```

```python
from contextlib import ExitStack

import concourse.bass as bass
from concourse import mybir
from concourse.bass import IndirectOffsetOnAxis

P = 128
QUAD = 32
NQ = P // QUAD
SMALL_ROWS = 1000
SMALL_ALL = 7
SMALL_LATER = 2
SMALL_PARTS = 125


def place_order(table_rows):
    small = [f for f, v in enumerate(table_rows) if v == SMALL_ROWS][:SMALL_ALL + SMALL_LATER]
    return small + [f for f in range(len(table_rows)) if f not in small]


def pair_slots(F):
    third = F // 3
    half = -(-third // 2)
    kinds = [(0, third, 2 * third), (2 * third, 0, third)]
    return [(2 * k + part, all0 + half * part, lead0 + half * part, lead, min(half, third - half * part))
            for k, (all0, lead0, lead) in enumerate(kinds) for part in range(2)]


def slot_count(F):
    return -(-(F // 3) // 2)


DENSE_QUADRANT = 1


def dlrm_tower(nc, dense_t, ids, small_ids, tables, w1p, w2, vectors, y):
    fp32 = mybir.dt.float32
    fp32r = mybir.dt.float32r
    i32 = mybir.dt.int32
    ALU = mybir.AluOpType
    ACT = mybir.ActivationFunctionType

    F = len(tables)
    ORDER = place_order([tb.shape[0] for tb in tables])
    NS = SMALL_ALL + SMALL_LATER
    D = tables[0].shape[1]
    B = ids.shape[0]
    TILES = B // P
    DENSE = dense_t.shape[0]
    SLOTS = slot_count(F)
    H1, H2 = w2.shape
    C1, C2 = H1 // P, H2 // P
    SR = SMALL_ROWS // SMALL_PARTS

    GROUPS = [[list(range(a, min(a + 4, F))) for a in range(NS if t else SMALL_ALL, F, 4)] for t in range(TILES)]
    GROUP_NO = {(t, g): n for n, (t, g) in enumerate((t, g) for t in range(TILES) for g in range(len(GROUPS[t])))}
    ROW_NO = {tp: n for n, tp in enumerate((t, p) for t in range(TILES) for g in GROUPS[t] for p in g)}

    WARM_UP = 11
    SETS = P // NQ
    CHUNK = 8
    CHUNKS = SETS // CHUNK

    def by_act(h, c):
        return 1 <= h < SMALL_ALL and c == SR - 1

    def made_before(h, c):
        made = [by_act(u, d) for u in range(h + 1) for d in range(SR) if (u, d) <= (h, c)]
        return len(made) - sum(made), sum(made)

    def first_tile(h):
        return 0 if h < SMALL_ALL else 1

    last = TILES - 1
    STEPS = []
    for h in range(SMALL_ALL):
        STEPS += [("small", h, None)]
        STEPS += [("rows", 0, h - 1)] if 1 <= h <= len(GROUPS[0]) else []
    halves = [("small", h, half) for h in range(SMALL_ALL, NS) for half in (0, 1)]
    STEPS += [halves[0], ("gram", 0, 0), halves[1], ("rows", 1, 0), ("gram", 0, 1), ("rows", 1, 1), ("rows", 1, 2)]
    STEPS += [("gram", 0, 2), ("gram", 0, 3), *halves[2:]]
    STEPS += [("rows", 1, g) for g in range(3, len(GROUPS[1]))]
    for t in range(1, last):
        STEPS += [("first", t - 1, 0)]
        STEPS += [("rows", t, len(GROUPS[t]) - 1)] if t >= 2 else []
        for k in range(CHUNKS):
            STEPS += [("first", t - 1, k + 1)] if k + 1 < C1 else []
            STEPS += [("gram", t, k)]
        STEPS += [("second", t - 1, None), ("rows", t + 1, 0), ("rows", t + 1, 1), ("third", t - 1, None)]
        STEPS += [("rows", t + 1, g) for g in range(2, len(GROUPS[t + 1]) - (2 if t + 1 == last else 1))]
    STEPS += [("first", last - 1, c) for c in range(C1 - 1)]
    STEPS += [("rows", last, g) for g in range(len(GROUPS[last]) - 2, len(GROUPS[last]))]
    STEPS += [("first", last - 1, C1 - 1)]
    STEPS += [("gram", last, k) for k in range(CHUNKS)]
    STEPS += [("second", last - 1, None), ("first", last, 0), ("third", last - 1, None)]
    STEPS += [("first", last, c) for c in range(1, C1)]
    STEPS += [("second", last, None), ("third", last, None)]

    with ExitStack() as ctx:
        def sb(name, shape, dt=fp32):
            return ctx.enter_context(nc.sbuf_tensor(name, shape, dt))

        def pb(name, shape):
            return ctx.enter_context(nc.psum_tensor(name, shape, fp32))

        def sem(name):
            return ctx.enter_context(nc.semaphore(name))

        ids_sb = sb("ids_sb", [P, TILES, F], i32)
        ident = sb("ident", [P, P])
        small_row_i = sb("small_row_i", [P, SR], i32)
        small_row = sb("small_row", [P, SR])
        minus_last_row = sb("minus_last_row", [P, 1])
        distance = sb("distance", [SMALL_PARTS, B])
        small_ids_sb = sb("small_ids_sb", [SMALL_PARTS, NS, B], i32)
        TABLES = 3
        table = sb("table", [SMALL_PARTS, TABLES, SR, D])
        table_hi = sb("table_hi", [SMALL_PARTS, 2, SR, D], fp32r)
        table_lo = sb("table_lo", [SMALL_PARTS, 2, SR, D], fp32r)
        RING = 12
        onehot = sb("onehot", [SMALL_PARTS, RING, B], fp32r)
        rows = sb("rows", [P, len(ROW_NO), D])
        emb_t = sb("emb_t", [D, TILES, SETS, NQ, QUAD])
        pairs = sb("pairs", [P, 2, SLOTS, P])
        w1_sb = sb("w1_sb", [P, SLOTS, H1])
        w2_sb = sb("w2_sb", [P, C1, H2])
        vectors_sb = sb("vectors_sb", [P, C1 + 2 * C2])
        b1_sb, b2_sb, w3_sb = vectors_sb[:, :C1], vectors_sb[:, C1:C1 + C2], vectors_sb[:, C1 + C2:]
        h1 = sb("h1", [P, C1, P])
        h2 = sb("h2", [P, C2, P])
        y_sb = sb("y_sb", [1, B])

        rows_t_banks = pb("rows_t_banks", [P, CHUNK, P])
        rows_t_ps = [rows_t_banks[:, k * (CHUNK // 2):(k + 1) * (CHUNK // 2), :].rearrange("p s x -> p (s x)")
                     for k in range(2)]
        gram_ps = [pb(f"gram_ps{k}", [P, CHUNK, P]) for k in range(2)]
        h1_ps = pb("h1_ps", [P, 512])
        h2_ps = pb("h2_ps", [P, 512])
        y_ps = h2_ps[0:1, C2 * P:(C2 + 1) * P]
        free_ps = [rows_t_ps[0], rows_t_ps[1], gram_ps[1].rearrange("p s x -> p (s x)")]

        def gram_out(t, k):
            if t == TILES - 1 and k >= 2:
                return rows_t_banks if k == 2 else gram_ps[0]
            return gram_ps[k % 2]

        def moved_before_gram(t, k):
            n = t * CHUNKS + k
            return n - 2 if t == TILES - 1 and k == 3 else n - 1

        def h1_out(t, c):
            return free_ps[c - 1][:, 0:P] if t == TILES - 1 and c else h1_ps[:, c * P:(c + 1) * P]

        def h2_out(t, c):
            return free_ps[c - 1][:, 0:P] if t == TILES - 1 and c else h2_ps[:, c * P:(c + 1) * P]

        small_ps = [h1_ps, h2_ps]

        ids_in = sem("ids_in")
        small_ids_in = [sem(f"small_ids_in{k}") for k in range(TABLES)]
        table_in = [sem(f"table_in{k}") for k in range(TABLES)]
        dense_in = sem("dense_in")
        w1_in = sem("w1_in")
        w2_in = sem("w2_in")
        vectors_in = sem("vectors_in")
        ident_clear = sem("ident_clear")
        ident_ready = sem("ident_ready")
        small_row_made = sem("small_row_made")
        small_row_ready = sem("small_row_ready")
        table_hi_ready = sem("table_hi_ready")
        table_lo_ready = sem("table_lo_ready")
        onehot_by_dve = sem("onehot_by_dve")
        onehot_by_act = sem("onehot_by_act")
        distance_ready = sem("distance_ready")
        onehot_used = sem("onehot_used")
        small_moved = sem("small_moved")
        gathered = {tg: sem(f"gathered_{tg[0]}_{tg[1]}") for tg in GROUP_NO}
        padded = sem("padded")
        rows_transposed = sem("rows_transposed")
        rows_moved = sem("rows_moved")
        gram_done = sem("gram_done")
        dve_over_all = sem("dve_over_all")
        act_over_all = sem("act_over_all")
        pairs_by_dve = sem("pairs_by_dve")
        pairs_by_act = sem("pairs_by_act")
        h1_done = sem("h1_done")
        h1_ready = sem("h1_ready")
        h1_end_by_dve = sem("h1_end_by_dve")
        h2_done = sem("h2_done")
        h2_ready = sem("h2_ready")
        h2_end_by_dve = sem("h2_end_by_dve")
        y_done = sem("y_done")
        y_ready = sem("y_ready")
        y_out = sem("y_out")

        def move_pairs(engine, engine_copy, over_all, moved, t, k, quadrants):
            n = t * CHUNKS + k
            for leading in (False, True):
                if leading:
                    engine.wait_ge(over_all, n + 1)
                for q in quadrants:
                    for r, all0, lead0, lead, count in pair_slots(F):
                        col, height = (lead0, lead) if leading else (all0, QUAD)
                        x0 = q * F + col
                        src = gram_out(t, k)[QUAD * q:QUAD * q + height, :, x0:x0 + count]
                        a = QUAD * q + k * CHUNK
                        dst = pairs[QUAD * r:QUAD * r + height, t % 2, 0:count, a:a + CHUNK]
                        last = engine_copy(dst, src.rearrange("p s j -> p j s"))
                last.then_inc(moved if leading else over_all, 1)

        def dve_quadrants(t, k):
            return (0,) if (k < CHUNKS - 1 if t == 0 else k == 1) else (0, 1)

        def act_quadrants(t, k):
            return tuple(q for q in range(NQ) if q not in dve_quadrants(t, k))

        block = ctx.enter_context(nc.Block())

        @block.sync
        def _(sp):
            sp.dma_start(ids_sb[:], ids.rearrange("(t p) f -> p t f", p=P)).then_inc(ids_in, 16)

            def load_table(h):
                if h >= TABLES:
                    sp.wait_ge(table_hi_ready, h - TABLES + 1)
                    sp.wait_ge(table_lo_ready, h - TABLES + 1)
                    sp.wait_ge(small_ids_in[h % TABLES], 16 * (h // TABLES))
                sp.dma_start(small_ids_sb[:, h, :], small_ids[h:h + 1, :].to_broadcast([SMALL_PARTS, B])
                             ).then_inc(small_ids_in[h % TABLES], 16)
                sp.dma_start(table[:, h % TABLES], tables[ORDER[h]].rearrange("(p c) d -> p c d", c=SR)
                             ).then_inc(table_in[h % TABLES], 16)

            def load_dense(t):
                rows0 = QUAD * DENSE_QUADRANT
                sp.dma_start(pairs[rows0:rows0 + DENSE, t % 2, SLOTS - 1, :], dense_t[:, t * P:(t + 1) * P]
                             ).then_inc(dense_in, 16)

            for h in range(TABLES):
                load_table(h)
            sp.dma_start(vectors_sb[:], vectors).then_inc(vectors_in, 16)
            sp.wait_ge(padded, 1)
            for t in range(2):
                load_dense(t)
            for h in range(TABLES, NS):
                load_table(h)
            sp.wait_ge(gram_done, 1)
            sp.dma_start(w1_sb[:], w1p.rearrange("s p n -> p s n")).then_inc(w1_in, 16)
            sp.dma_start(w2_sb[:], w2.rearrange("(c p) n -> p c n", p=P)).then_inc(w2_in, 16)
            for t in range(2, TILES):
                sp.wait_ge(h1_done, t - 1)
                sp.wait_ge(dense_in, 16 * t)
                load_dense(t)
            sp.wait_ge(y_ready, TILES)
            sp.dma_start(y, y_sb[:]).then_inc(y_out, 16)
            sp.wait_ge(y_out, 16)

        @block.gpsimd
        def _(pool):
            nc.gpsimd.iota(small_row_i[:], pattern=[[1, SR]], base=0, channel_multiplier=SR
                           ).then_inc(small_row_made, 1)
            nc.gpsimd.memset(ident[:], 0.0).then_inc(ident_clear, 1)
            pool.wait_ge(ident_clear, 1)
            nc.gpsimd.affine_select(out=ident[:], in_=ident[:], compare_op=ALU.not_equal, fill=1.0, base=0,
                                    pattern=[[-1, P]], channel_multiplier=1).then_inc(ident_ready, 1)
            pool.wait_ge(ids_in, 16)
            for t, g in GROUP_NO:
                for p in GROUPS[t][g]:
                    f = ORDER[p]
                    nc.gpsimd.indirect_dma_start(
                        rows[:, ROW_NO[t, p], :], None, tables[f],
                        IndirectOffsetOnAxis(ap=ids_sb[:, t, f:f + 1], axis=0),
                    ).then_inc(gathered[t, g], 16)

        @block.tensor
        def _(pe):
            def pick_small_rows(h, half):
                out = small_ps[h % 2][:, first_tile(h) * P:B]
                if h >= 2 and half != 1:
                    pe.wait_ge(small_moved, h - 1)
                both = ((table_hi, table_hi_ready), (table_lo, table_lo_ready))
                passes = [both] if h else [both[:1], both[1:]]
                for turn in passes:
                    for c in range(SR // 2 if half == 1 else 0, SR // 2 if half == 0 else SR):
                        n = h * SR + c
                        if by_act(h, c):
                            pe.wait_ge(onehot_by_act, made_before(h, c)[1])
                        else:
                            pe.wait_ge(onehot_by_dve, made_before(h, c)[0])
                        for part, ready in turn:
                            if c == 0:
                                pe.wait_ge(ready, h + 1)
                            last = nc.tensor.matmul(out, part[:, h % 2, c, :],
                                                    onehot[:, n % RING, 0:B - first_tile(h) * P],
                                                    start=(c == 0 and part is table_hi),
                                                    stop=(c == SR - 1 and part is table_lo))
                        if turn is passes[-1]:
                            last.then_inc(onehot_used, 1)

            def transpose_rows(t, g):
                n = GROUP_NO[t, g]
                pe.wait_ge(gathered[t, g], 16 * len(GROUPS[t][g]))
                if n >= 2:
                    pe.wait_ge(rows_moved, n - 1)
                for k, p in enumerate(GROUPS[t][g]):
                    last = nc.tensor.transpose(rows_t_ps[n % 2][:, k * P:(k + 1) * P],
                                               rows[:, ROW_NO[t, p], :], ident[:])
                last.then_inc(rows_transposed, 1)

            def gram(t, k):
                n = t * CHUNKS + k
                if k == 0:
                    pe.wait_ge(small_moved, SMALL_ALL if t == 0 else NS)
                    pe.wait_ge(rows_moved, GROUP_NO[t, len(GROUPS[t]) - 1] + 1)
                if n >= 2 and gram_out(t, k) is not rows_t_banks:
                    pe.wait_ge(pairs_by_dve, moved_before_gram(t, k))
                    pe.wait_ge(pairs_by_act, moved_before_gram(t, k))
                for s in range(CHUNK):
                    four = emb_t[:, t, k * CHUNK + s, :, :]
                    last = nc.tensor.matmul(gram_out(t, k)[:, s, 0:NQ * F], four.rearrange("d q f -> d (q f)"),
                                            four[:, :, 0:F], start=True, stop=True)
                last.then_inc(gram_done, 1)

            def first_layer(t, c):
                if c == 0:
                    pe.wait_ge(pairs_by_dve, CHUNKS * (t + 1))
                    pe.wait_ge(pairs_by_act, CHUNKS * (t + 1))
                    pe.wait_ge(dense_in, 16 * max(t + 1, 2))
                    if t == 0:
                        pe.wait_ge(w1_in, 16)
                        pe.wait_ge(small_moved, NS)
                    else:
                        pe.wait_ge(h1_ready, t)
                for s in range(SLOTS):
                    last = nc.tensor.matmul(h1_out(t, c), w1_sb[:, s, c * P:(c + 1) * P],
                                            pairs[:, t % 2, s, :], start=(s == 0), stop=(s == SLOTS - 1))
                if c == C1 - 1 or t == TILES - 1:
                    last.then_inc(h1_done, 1)

            def second_layer(t):
                pe.wait_ge(h1_ready, t + 1)
                if t == 0:
                    pe.wait_ge(w2_in, 16)
                    pe.wait_ge(vectors_in, 16)
                else:
                    pe.wait_ge(y_ready, t)
                for c in range(C2):
                    for k in range(C1):
                        if t == TILES - 1 and k == C1 - 1 and c == 0:
                            pe.wait_ge(h1_end_by_dve, 1)
                        last = nc.tensor.matmul(h2_out(t, c), w2_sb[:, k, c * P:(c + 1) * P],
                                                h1[:, k, :], start=(k == 0), stop=(k == C1 - 1))
                    if c == C2 - 1 or t == TILES - 1:
                        last.then_inc(h2_done, 1)

            def third_layer(t):
                pe.wait_ge(h2_ready, t + 1)
                for k in range(C2):
                    if t == TILES - 1 and k == C2 - 1:
                        pe.wait_ge(h2_end_by_dve, 1)
                    last = nc.tensor.matmul(y_ps, w3_sb[:, k:k + 1], h2[:, k, :],
                                            start=(k == 0), stop=(k == C2 - 1))
                last.then_inc(y_done, 1)

            pe.wait_ge(ident_ready, 1)
            for _ in range(WARM_UP):
                nc.tensor.matmul(rows_t_ps[0][:, 0:P], ident[:], ident[:], start=True, stop=True)
            pe.wait_ge(padded, 1)
            for what, n, k in STEPS:
                if what == "small":
                    pick_small_rows(n, k)
                elif what == "rows":
                    transpose_rows(n, k)
                elif what == "gram":
                    gram(n, k)
                elif what == "first":
                    first_layer(n, k)
                elif what == "second":
                    second_layer(n)
                else:
                    third_layer(n)

        @block.vector
        def _(dve):
            nc.vector.memset(emb_t[:, :, :, :, F:QUAD].rearrange("d t s q f -> d (t s q) f"), 0.0)
            nc.vector.memset(pairs[:, :, SLOTS - 1, :], 0.0).then_inc(padded, 1)
            dve.wait_ge(small_row_made, 1)
            nc.vector.tensor_scalar(minus_last_row[:], small_row_i[:, SR - 1:SR], -1.0, None, ALU.mult)
            nc.vector.tensor_copy(small_row[:], small_row_i[:]).then_inc(small_row_ready, 1)
            dve.wait_ge(small_row_ready, 1)
            dve.wait_ge(padded, 1)

            def table_rest(h):
                dve.wait_ge(table_hi_ready, h + 1)
                nc.vector.tensor_tensor(table_lo[:, h % 2], table[:, h % TABLES], table_hi[:, h % 2].bitcast(fp32),
                                        ALU.subtract).then_inc(table_lo_ready, 1)

            def small_onehot(h):
                samples = slice(first_tile(h) * P, B)
                dve.wait_ge(small_ids_in[h % TABLES], 16 * (h // TABLES + 1))
                for c in range(SR):
                    if by_act(h, c):
                        continue
                    n = h * SR + c
                    if n >= RING:
                        dve.wait_ge(onehot_used, n - RING + 1)
                    nc.vector.tensor_scalar(onehot[:, n % RING, 0:B - first_tile(h) * P],
                                            small_ids_sb[:, h, samples], small_row[0:SMALL_PARTS, c:c + 1],
                                            None, ALU.is_equal).then_inc(onehot_by_dve, 1)
                    if c == (0 if h else SR - 1):
                        table_rest(h)

            for what, n, k in STEPS:
                if what == "small" and n < NS - 1 and k != 1:
                    small_onehot(n)
                elif what == "gram":
                    if n == 0 and k == 0:
                        small_onehot(NS - 1)
                    if k == 0 and n >= 2:
                        dve.wait_ge(h1_done, n - 1)
                    dve.wait_ge(gram_done, n * CHUNKS + k + 1)
                    move_pairs(dve, nc.vector.tensor_copy, dve_over_all, pairs_by_dve, n, k, dve_quadrants(n, k))

            dve.wait_ge(vectors_in, 16)
            dve.wait_ge(h2_done, TILES - 1)
            dve.wait_ge(h1_done, TILES - 1 + C1)
            nc.vector.tensor_scalar(h1[:, C1 - 1, :], h1_out(TILES - 1, C1 - 1), b1_sb[:, C1 - 1:C1], 0.0,
                                    ALU.add, ALU.max).then_inc(h1_end_by_dve, 1)
            dve.wait_ge(y_done, TILES - 1)
            dve.wait_ge(h2_done, TILES - 1 + C2)
            nc.vector.tensor_scalar(h2[:, C2 - 1, :], h2_out(TILES - 1, C2 - 1), b2_sb[:, C2 - 1:C2], 0.0,
                                    ALU.add, ALU.max).then_inc(h2_end_by_dve, 1)

        @block.scalar
        def _(act):
            def table_high(h):
                act.wait_ge(table_in[h % TABLES], 16 * (h // TABLES + 1))
                if h >= 2:
                    act.wait_ge(onehot_used, SR * (h - 1))
                nc.scalar.copy(table_hi[:, h % 2], table[:, h % TABLES]).then_inc(table_hi_ready, 1)

            def small_onehot_last(h):
                n = h * SR + SR - 1
                samples = slice(first_tile(h) * P, B)
                width = B - first_tile(h) * P
                act.wait_ge(small_ids_in[h % TABLES], 16 * (h // TABLES + 1))
                nc.scalar.activation(distance[:, 0:width], small_ids_sb[:, h, samples], ACT.Abs,
                                     bias=minus_last_row[0:SMALL_PARTS, :]).then_inc(distance_ready, 1)
                act.wait_ge(distance_ready, h)
                act.wait_ge(onehot_used, n - RING + 1)
                nc.scalar.activation(onehot[:, n % RING, 0:width], distance[:, 0:width], ACT.Relu,
                                     bias=1.0, scale=-1.0).then_inc(onehot_by_act, 1)

            def move_small_rows(h):
                act.wait_ge(onehot_used, SR * (h + 1))
                t0 = first_tile(h)
                nc.scalar.copy(emb_t[:, t0:, :, :, h].rearrange("d t s q -> d t q s"),
                               small_ps[h % 2][:, t0 * P:B].rearrange("d (t q s) -> d t q s", t=TILES - t0, q=NQ)
                               ).then_inc(small_moved, 1)

            def move_rows(t, g):
                places = GROUPS[t][g]
                n = GROUP_NO[t, g]
                act.wait_ge(rows_transposed, n + 1)
                nc.scalar.copy(
                    emb_t[:, t, :, :, places[0]:places[-1] + 1].rearrange("d s q f -> d f q s"),
                    rows_t_ps[n % 2][:, 0:len(places) * P].rearrange("d (f q s) -> d f q s", f=len(places), q=NQ)
                ).then_inc(rows_moved, 1)

            def move_h1(t):
                act.wait_ge(h1_done, t + 1)
                if t == 0:
                    act.wait_ge(vectors_in, 16)
                else:
                    act.wait_ge(h2_done, t)
                for c in range(C1 - 1 if t == TILES - 1 else C1):
                    if t == TILES - 1:
                        act.wait_ge(h1_done, t + 1 + c)
                    last = nc.scalar.activation(h1[:, c, :], h1_out(t, c), ACT.Relu, bias=b1_sb[:, c:c + 1])
                last.then_inc(h1_ready, 1)

            def move_h2(t):
                act.wait_ge(h2_done, t + 1)
                if t >= 1:
                    act.wait_ge(y_done, t)
                for c in range(C2 - 1 if t == TILES - 1 else C2):
                    last = nc.scalar.activation(h2[:, c, :], h2_out(t, c), ACT.Relu, bias=b2_sb[:, c:c + 1])
                last.then_inc(h2_ready, 1)

            table_high(0)
            act.wait_ge(padded, 1)
            table_high(1)
            for what, n, k in STEPS:
                if what == "small" and k != 0:
                    move_small_rows(n)
                    if n + 2 < NS and n + 1 != SMALL_ALL:
                        table_high(n + 2)
                    if n + 1 < SMALL_ALL:
                        small_onehot_last(n + 1)
                elif what == "small":
                    if n == SMALL_ALL:
                        table_high(n + 1)
                elif what == "rows":
                    move_rows(n, k)
                elif what == "gram":
                    if k == 0 and n >= 2:
                        act.wait_ge(h1_done, n - 1)
                    act.wait_ge(gram_done, n * CHUNKS + k + 1)
                    move_pairs(act, nc.scalar.copy, act_over_all, pairs_by_act, n, k, act_quadrants(n, k))
                elif what == "first" and k == C1 - 1:
                    move_h1(n)
                elif what == "second":
                    move_h2(n)
                elif what == "third":
                    act.wait_ge(y_done, n + 1)
                    nc.scalar.copy(y_sb[:, n * P:(n + 1) * P], y_ps).then_inc(y_ready, 1)


def first_layer_rows(w1, order):
    import numpy as np

    F = len(order)
    pair_row = np.full((F, F), -1)
    i, j = np.triu_indices(F, k=1)
    pair_row[i, j] = pair_row[j, i] = np.arange(len(i))
    out = np.zeros((slot_count(F), NQ, QUAD, w1.shape[1]), w1.dtype)
    for r, all0, lead0, lead, count in pair_slots(F):
        for s in range(count):
            for row in range(F):
                col = (lead0 if row < lead else all0) + s
                third = F // 3
                if row // third != col // third or row < col:
                    out[s, r, row] = w1[pair_row[order[row], order[col]]]
    out[-1, DENSE_QUADRANT, :w1.shape[0] - len(i)] = w1[len(i):]
    return out.reshape(out.shape[0], P, -1)


def kernel(**inputs):
    import numpy as np
    import concourse.bacc as bacc
    from concourse.bass_utils import run_bass_kernel_spmd

    F = inputs["ids"].shape[1]
    order = place_order([inputs[f"tbl_{f}"].shape[0] for f in range(F)])
    ids = np.asarray(inputs["ids"])
    laid = {"dense_t": np.ascontiguousarray(np.asarray(inputs["dense_ctx"]).T),
            "ids": np.ascontiguousarray(ids),
            "small_ids": np.ascontiguousarray(ids.T[order[:SMALL_ALL + SMALL_LATER]]),
            **{f"tbl_{f}": np.ascontiguousarray(inputs[f"tbl_{f}"]) for f in range(F)},
            "w1p": first_layer_rows(np.asarray(inputs["W_top1"]), order),
            "w2": np.ascontiguousarray(inputs["W_top2"]),
            "vectors": np.concatenate([np.asarray(inputs[k]).reshape(-1, P)
                                       for k in ("b_top1", "b_top2", "W_top3")]).T.copy()}

    nc = bacc.Bacc("TRN2", target_bir_lowering=False, num_devices=1)
    ap = {k: nc.dram_tensor(k + "_dram", v.shape, mybir.dt.from_np(v.dtype), kind="ExternalInput").ap()
          for k, v in laid.items()}
    B = laid["ids"].shape[0]
    y = nc.dram_tensor("y_dram", (1, B), mybir.dt.float32, kind="ExternalOutput").ap()
    dlrm_tower(nc, ap["dense_t"], ap["ids"], ap["small_ids"], [ap[f"tbl_{f}"] for f in range(F)], ap["w1p"],
               ap["w2"], ap["vectors"], y)
    r = run_bass_kernel_spmd(nc, [{k + "_dram": v for k, v in laid.items()}], core_ids=[0])
    return r.results[0]["y_dram"].reshape(B, 1)
```
